# Optimizing a Trainium2 kernel written in Bass

```python
import numpy as np
import jax
import jax.numpy as jnp

def _softmax(x, axis=-1):
    return jax.nn.softmax(x, axis=axis)

def _gelu(x):
    return jax.nn.gelu(x, approximate=True)

def _silu(x):
    return jax.nn.silu(x)

def _sigmoid(x):
    return jax.nn.sigmoid(x)

def _layernorm(x, axis=-1, eps=1e-05):
    m = jnp.mean(x, axis=axis, keepdims=True)
    v = jnp.var(x, axis=axis, keepdims=True)
    return (x - m) / jnp.sqrt(v + eps)

def _scatter_add(tgt, idx, src, axis=0):
    return tgt.at[idx].add(src)

def _segment_sum(src, seg, n):
    return jax.ops.segment_sum(src, seg, n)
kernel_name = 'mk_hybrid_d1_jaxref_r8_84e0f1'

def setup_inputs(seed: int=0):
    np.random.seed(seed)
    _w = jnp.asarray

    def _L0_attn_a_setup():
        import jax, jax.numpy as jnp
        import numpy as np
        B, L, H, N = (4, 512, 128, 64)
        LK = 64

        def _dss_kernel(Lambda_re, Lambda_im, log_dt, W_re, W_im, Lk):
            dt = jnp.exp(log_dt)
            Lam = -jnp.exp(Lambda_re) + 1j * Lambda_im
            dtLam = dt[:, None] * Lam[None, :]
            P = dtLam[:, :, None] * jnp.arange(Lk, dtype=jnp.float32)
            S = jnp.exp(P)
            W = W_re + 1j * W_im
            k = jnp.einsum('hn,hnl->lh', W, S).real
            return k
        key = jax.random.key(seed)
        ks = jax.random.split(key, 7)
        u = jax.random.normal(ks[0], (B, L, H), jnp.float32)
        D = jax.random.normal(ks[1], (H,), jnp.float32)
        Lambda_re = jax.random.normal(ks[2], (N,), jnp.float32) * 0.5
        Lambda_im = jax.random.normal(ks[3], (N,), jnp.float32) * np.pi
        log_dt = jax.random.uniform(ks[4], (H,), jnp.float32, minval=np.log(0.001), maxval=np.log(0.1))
        W_re = jax.random.normal(ks[5], (H, N), jnp.float32) / np.sqrt(N)
        W_im = jax.random.normal(ks[6], (H, N), jnp.float32) / np.sqrt(N)
        return dict(u=u, D=D, Lambda_re=Lambda_re, Lambda_im=Lambda_im, log_dt=log_dt, W_re=W_re, W_im=W_im)
    _L0_attn_a_in = _L0_attn_a_setup()

    def _L0_attn_b_setup():
        import jax, jax.numpy as jnp
        import numpy as np
        EMBED = 128
        HEADS = 16
        SPARSITY = 4
        B, S = (2, 256)

        def _mask(seq_len):
            i = jnp.arange(seq_len)[:, None]
            j = jnp.arange(seq_len)[None, :]
            upper = j > i
            return upper | upper & ((j - i) % SPARSITY != 0)
        key = jax.random.key(seed)
        k0, k1, k2, k3, k4 = jax.random.split(key, 5)
        E = EMBED
        x = jax.random.normal(k0, (B, S, E), jnp.float32)
        in_proj_w = jax.random.normal(k1, (3 * E, E), jnp.float32) * E ** (-0.5)
        in_proj_b = jax.random.normal(k2, (3 * E,), jnp.float32) * 0.02
        out_proj_w = jax.random.normal(k3, (E, E), jnp.float32) * E ** (-0.5)
        out_proj_b = jax.random.normal(k4, (E,), jnp.float32) * 0.02
        return {'x': x, 'in_proj_w': in_proj_w, 'in_proj_b': in_proj_b, 'out_proj_w': out_proj_w, 'out_proj_b': out_proj_b}
    _L0_attn_b_in = _L0_attn_b_setup()

    def _L0_ffn_setup():
        import jax, jax.numpy as jnp
        import numpy as np
        DIM = 128
        DEPTH = 6
        HEADS = 16
        DIM_HEAD = 64
        WINDOW = 32
        INNER = HEADS * DIM_HEAD
        DIM_INNER = int(DIM * 4 * 2 / 3)
        QK_SCALE = 8.0

        def shift_tokens(t):
            a, s = jnp.split(t, 2, -1)
            s = jnp.pad(s, ((0, 0), (1, 0), (0, 0)))[:, :-1]
            return jnp.concatenate([a, s], -1)

        def l2norm(t):
            return t / jnp.maximum(jnp.linalg.norm(t, axis=-1, keepdims=True), 1e-12)

        def rotate_half(x):
            x1, x2 = jnp.split(x, 2, -1)
            return jnp.concatenate([-x2, x1], -1)

        def rotary_tables(n):
            half = jnp.arange(0, DIM_HEAD, 2, dtype=jnp.float32)
            inv_freq = 1.0 / 10000.0 ** (half / DIM_HEAD)
            t = jnp.arange(n, dtype=jnp.float32)
            freqs = t[:, None] * inv_freq[None, :]
            freqs = jnp.concatenate([freqs, freqs], -1)
            base_scale = (half + 0.4 * DIM_HEAD) / (1.4 * DIM_HEAD)
            power = (t - n // 2) / (WINDOW // 2)
            scale = base_scale[None, :] ** power[:, None]
            scale = jnp.concatenate([scale, scale], -1)
            return (freqs, scale)

        def local_attention(q, k, v):
            b, h, n, d = q.shape
            w = WINDOW
            nw = n // w
            bq = q.reshape(b, h, nw, w, d)
            bk = k.reshape(b, h, nw, w, d)
            bv = v.reshape(b, h, nw, w, d)

            def look(t):
                p = jnp.pad(t, ((0, 0), (0, 0), (1, 0), (0, 0), (0, 0)))
                return jnp.concatenate([p[:, :, :nw], p[:, :, 1:]], axis=3)
            bk2, bv2 = (look(bk), look(bv))
            seq = jnp.arange(n).reshape(nw, w)
            seq_p = jnp.pad(seq, ((1, 0), (0, 0)), constant_values=-1)
            jt = jnp.concatenate([seq_p[:nw], seq_p[1:]], axis=1)
            it = seq[:, :, None]
            jb = jt[:, None, :]
            mask = (it < jb) | (it > jb + w) | (jb == -1)
            sim = jnp.einsum('bhwie,bhwje->bhwij', bq, bk2) * QK_SCALE
            sim = jnp.where(mask, -jnp.finfo(sim.dtype).max, sim)
            attn = jax.nn.softmax(sim, -1)
            out = jnp.einsum('bhwij,bhwje->bhwie', attn, bv2)
            return out.reshape(b, h, n, d)

        def attn_layer(x, Wqkv, qs, ksc, Wo):
            b, n, _ = x.shape
            qkv = x @ Wqkv
            q, k, v = jnp.split(qkv, 3, -1)
            sh = lambda t: t.reshape(b, n, HEADS, DIM_HEAD).transpose(0, 2, 1, 3)
            q, k, v = (sh(q), sh(k), sh(v))
            q = l2norm(q) * qs
            k = l2norm(k) * ksc
            freqs, scale = rotary_tables(n)
            cos, sin = (jnp.cos(freqs), jnp.sin(freqs))
            q = q * cos * scale + rotate_half(q) * sin * scale
            inv = 1.0 / scale
            k = k * cos * inv + rotate_half(k) * sin * inv
            out = local_attention(q, k, v)
            out = out.transpose(0, 2, 1, 3).reshape(b, n, INNER)
            return out @ Wo

        def ffn_layer(x, g, bln, W1, b1, W2, b2):
            mu = x.mean(-1, keepdims=True)
            var = ((x - mu) ** 2).mean(-1, keepdims=True)
            xn = (x - mu) / jnp.sqrt(var + 1e-05) * g + bln
            hg = xn @ W1 + b1
            a, gate = jnp.split(hg, 2, -1)
            return a * jax.nn.gelu(gate, approximate=False) @ W2 + b2
        key = jax.random.key(seed)
        ks = jax.random.split(key, 8)
        B, N = (2, 256)
        init = lambda k, shape: jax.random.normal(k, shape, jnp.float32) * 0.02
        return {'x': jax.random.normal(ks[0], (B, N, DIM), jnp.float32), 'Wqkv': init(ks[1], (DEPTH, DIM, 3 * INNER)), 'q_scale': jnp.ones((DEPTH, DIM_HEAD), jnp.float32), 'k_scale': jnp.ones((DEPTH, DIM_HEAD), jnp.float32), 'Wo': init(ks[2], (DEPTH, INNER, DIM)), 'ln_g': jnp.ones((DEPTH, DIM), jnp.float32), 'ln_b': jnp.zeros((DEPTH, DIM), jnp.float32), 'W1': init(ks[3], (DEPTH, DIM, 2 * DIM_INNER)), 'b1': jnp.zeros((DEPTH, 2 * DIM_INNER), jnp.float32), 'W2': init(ks[4], (DEPTH, DIM_INNER, DIM)), 'b2': jnp.zeros((DEPTH, DIM), jnp.float32)}
    _L0_ffn_in = _L0_ffn_setup()
    _d = {'L0_attn_a_u': _L0_attn_a_in['u'], 'L0_attn_a_D': _L0_attn_a_in['D'], 'L0_attn_a_Lambda_re': _L0_attn_a_in['Lambda_re'], 'L0_attn_a_Lambda_im': _L0_attn_a_in['Lambda_im'], 'L0_attn_a_log_dt': _L0_attn_a_in['log_dt'], 'L0_attn_a_W_re': _L0_attn_a_in['W_re'], 'L0_attn_a_W_im': _L0_attn_a_in['W_im'], 'L0_attn_b_in_proj_w': _L0_attn_b_in['in_proj_w'], 'L0_attn_b_in_proj_b': _L0_attn_b_in['in_proj_b'], 'L0_attn_b_out_proj_w': _L0_attn_b_in['out_proj_w'], 'L0_attn_b_out_proj_b': _L0_attn_b_in['out_proj_b'], 'L0_ffn_Wqkv': _L0_ffn_in['Wqkv'], 'L0_ffn_q_scale': _L0_ffn_in['q_scale'], 'L0_ffn_k_scale': _L0_ffn_in['k_scale'], 'L0_ffn_Wo': _L0_ffn_in['Wo'], 'L0_ffn_ln_g': _L0_ffn_in['ln_g'], 'L0_ffn_ln_b': _L0_ffn_in['ln_b'], 'L0_ffn_W1': _L0_ffn_in['W1'], 'L0_ffn_b1': _L0_ffn_in['b1'], 'L0_ffn_W2': _L0_ffn_in['W2'], 'L0_ffn_b2': _L0_ffn_in['b2']}
    _x0 = _d['L0_attn_a_u']
    _d['L0_attn_a_u'] = jax.random.normal(jax.random.fold_in(jax.random.key(seed), 1), (1, 2048, 128), dtype=_x0.dtype)
    del _x0
    return _d

def reference(L0_attn_a_u, L0_attn_a_D, L0_attn_a_Lambda_re, L0_attn_a_Lambda_im, L0_attn_a_log_dt, L0_attn_a_W_re, L0_attn_a_W_im, L0_attn_b_in_proj_w, L0_attn_b_in_proj_b, L0_attn_b_out_proj_w, L0_attn_b_out_proj_b, L0_ffn_Wqkv, L0_ffn_q_scale, L0_ffn_k_scale, L0_ffn_Wo, L0_ffn_ln_g, L0_ffn_ln_b, L0_ffn_W1, L0_ffn_b1, L0_ffn_W2, L0_ffn_b2):

    def _L0_attn_a_ref(u, D, Lambda_re, Lambda_im, log_dt, W_re, W_im):
        import jax, jax.numpy as jnp
        import numpy as np
        B, L, H, N = (4, 512, 128, 64)
        LK = 64

        def _dss_kernel(Lambda_re, Lambda_im, log_dt, W_re, W_im, Lk):
            dt = jnp.exp(log_dt)
            Lam = -jnp.exp(Lambda_re) + 1j * Lambda_im
            dtLam = dt[:, None] * Lam[None, :]
            P = dtLam[:, :, None] * jnp.arange(Lk, dtype=jnp.float32)
            S = jnp.exp(P)
            W = W_re + 1j * W_im
            k = jnp.einsum('hn,hnl->lh', W, S).real
            return k
        Lseq = u.shape[1]
        Lk = min(LK, Lseq)
        k = _dss_kernel(Lambda_re, Lambda_im, log_dt, W_re, W_im, Lk)
        n = Lseq + Lk
        k_f = jnp.fft.rfft(k, n=n, axis=0)
        u_f = jnp.fft.rfft(u, n=n, axis=1)
        y = jnp.fft.irfft(k_f[None, :, :] * u_f, n=n, axis=1)[:, :Lseq, :]
        return y + u * D[None, None, :]

    def _L0_attn_b_ref(x, in_proj_w, in_proj_b, out_proj_w, out_proj_b):
        import jax, jax.numpy as jnp
        import numpy as np
        EMBED = 128
        HEADS = 16
        SPARSITY = 4
        B, S = (2, 256)

        def _mask(seq_len):
            i = jnp.arange(seq_len)[:, None]
            j = jnp.arange(seq_len)[None, :]
            upper = j > i
            return upper | upper & ((j - i) % SPARSITY != 0)
        b, s, e = x.shape
        h = HEADS
        d = e // h
        qkv = x @ in_proj_w.T + in_proj_b
        q, k, v = jnp.split(qkv, 3, axis=-1)
        q = q.reshape(b, s, h, d)
        k = k.reshape(b, s, h, d)
        v = v.reshape(b, s, h, d)
        scores = jnp.einsum('bqhd,bkhd->bhqk', q, k) * d ** (-0.5)
        scores = jnp.where(_mask(s)[None, None], -jnp.inf, scores)
        attn = jax.nn.softmax(scores, axis=-1)
        ctx = jnp.einsum('bhqk,bkhd->bqhd', attn, v).reshape(b, s, e)
        return ctx @ out_proj_w.T + out_proj_b

    def _L0_ffn_ref(x, Wqkv, q_scale, k_scale, Wo, ln_g, ln_b, W1, b1, W2, b2):
        import jax, jax.numpy as jnp
        import numpy as np
        DIM = 128
        DEPTH = 6
        HEADS = 16
        DIM_HEAD = 64
        WINDOW = 32
        INNER = HEADS * DIM_HEAD
        DIM_INNER = int(DIM * 4 * 2 / 3)
        QK_SCALE = 8.0

        def shift_tokens(t):
            a, s = jnp.split(t, 2, -1)
            s = jnp.pad(s, ((0, 0), (1, 0), (0, 0)))[:, :-1]
            return jnp.concatenate([a, s], -1)

        def l2norm(t):
            return t / jnp.maximum(jnp.linalg.norm(t, axis=-1, keepdims=True), 1e-12)

        def rotate_half(x):
            x1, x2 = jnp.split(x, 2, -1)
            return jnp.concatenate([-x2, x1], -1)

        def rotary_tables(n):
            half = jnp.arange(0, DIM_HEAD, 2, dtype=jnp.float32)
            inv_freq = 1.0 / 10000.0 ** (half / DIM_HEAD)
            t = jnp.arange(n, dtype=jnp.float32)
            freqs = t[:, None] * inv_freq[None, :]
            freqs = jnp.concatenate([freqs, freqs], -1)
            base_scale = (half + 0.4 * DIM_HEAD) / (1.4 * DIM_HEAD)
            power = (t - n // 2) / (WINDOW // 2)
            scale = base_scale[None, :] ** power[:, None]
            scale = jnp.concatenate([scale, scale], -1)
            return (freqs, scale)

        def local_attention(q, k, v):
            b, h, n, d = q.shape
            w = WINDOW
            nw = n // w
            bq = q.reshape(b, h, nw, w, d)
            bk = k.reshape(b, h, nw, w, d)
            bv = v.reshape(b, h, nw, w, d)

            def look(t):
                p = jnp.pad(t, ((0, 0), (0, 0), (1, 0), (0, 0), (0, 0)))
                return jnp.concatenate([p[:, :, :nw], p[:, :, 1:]], axis=3)
            bk2, bv2 = (look(bk), look(bv))
            seq = jnp.arange(n).reshape(nw, w)
            seq_p = jnp.pad(seq, ((1, 0), (0, 0)), constant_values=-1)
            jt = jnp.concatenate([seq_p[:nw], seq_p[1:]], axis=1)
            it = seq[:, :, None]
            jb = jt[:, None, :]
            mask = (it < jb) | (it > jb + w) | (jb == -1)
            sim = jnp.einsum('bhwie,bhwje->bhwij', bq, bk2) * QK_SCALE
            sim = jnp.where(mask, -jnp.finfo(sim.dtype).max, sim)
            attn = jax.nn.softmax(sim, -1)
            out = jnp.einsum('bhwij,bhwje->bhwie', attn, bv2)
            return out.reshape(b, h, n, d)

        def attn_layer(x, Wqkv, qs, ksc, Wo):
            b, n, _ = x.shape
            qkv = x @ Wqkv
            q, k, v = jnp.split(qkv, 3, -1)
            sh = lambda t: t.reshape(b, n, HEADS, DIM_HEAD).transpose(0, 2, 1, 3)
            q, k, v = (sh(q), sh(k), sh(v))
            q = l2norm(q) * qs
            k = l2norm(k) * ksc
            freqs, scale = rotary_tables(n)
            cos, sin = (jnp.cos(freqs), jnp.sin(freqs))
            q = q * cos * scale + rotate_half(q) * sin * scale
            inv = 1.0 / scale
            k = k * cos * inv + rotate_half(k) * sin * inv
            out = local_attention(q, k, v)
            out = out.transpose(0, 2, 1, 3).reshape(b, n, INNER)
            return out @ Wo

        def ffn_layer(x, g, bln, W1, b1, W2, b2):
            mu = x.mean(-1, keepdims=True)
            var = ((x - mu) ** 2).mean(-1, keepdims=True)
            xn = (x - mu) / jnp.sqrt(var + 1e-05) * g + bln
            hg = xn @ W1 + b1
            a, gate = jnp.split(hg, 2, -1)
            return a * jax.nn.gelu(gate, approximate=False) @ W2 + b2
        for i in range(DEPTH):
            x = attn_layer(shift_tokens(x), Wqkv[i], q_scale[i], k_scale[i], Wo[i]) + x
            x = ffn_layer(shift_tokens(x), ln_g[i], ln_b[i], W1[i], b1[i], W2[i], b2[i]) + x
        return x
    x = L0_attn_a_u
    x = x + _L0_attn_a_ref(_layernorm(x, axis=-1), L0_attn_a_D, L0_attn_a_Lambda_re, L0_attn_a_Lambda_im, L0_attn_a_log_dt, L0_attn_a_W_re, L0_attn_a_W_im)
    x = x + _L0_ffn_ref(_layernorm(x, axis=-1), L0_ffn_Wqkv, L0_ffn_q_scale, L0_ffn_k_scale, L0_ffn_Wo, L0_ffn_ln_g, L0_ffn_ln_b, L0_ffn_W1, L0_ffn_b1, L0_ffn_W2, L0_ffn_b2)
    x = x + _L0_attn_b_ref(_layernorm(x, axis=-1), L0_attn_b_in_proj_w, L0_attn_b_in_proj_b, L0_attn_b_out_proj_w, L0_attn_b_out_proj_b)
    x = x + _L0_ffn_ref(_layernorm(x, axis=-1), L0_ffn_Wqkv, L0_ffn_q_scale, L0_ffn_k_scale, L0_ffn_Wo, L0_ffn_ln_g, L0_ffn_ln_b, L0_ffn_W1, L0_ffn_b1, L0_ffn_W2, L0_ffn_b2)
    return x

_drawn_inputs = setup_inputs


def setup_inputs(seed=0):
    import zlib

    import numpy as np

    out = dict(_drawn_inputs(seed))
    spreads = {'L0_ffn_q_scale': (1.0, 0.6),
     'L0_ffn_k_scale': (1.0, 0.6),
     'L0_ffn_ln_g': (1.0, 0.6),
     'L0_ffn_ln_b': (0.0, 0.8),
     'L0_ffn_b1': (0.0, 0.8),
     'L0_ffn_b2': (0.0, 0.296)}
    factors = {'L0_attn_b_in_proj_b': 54.816,
     'L0_attn_b_out_proj_b': 60.065,
     'L0_ffn_W1': 6.314,
     'L0_ffn_W2': 6.218}
    for name, (base, spread) in spreads.items():
        noise = np.random.default_rng([zlib.crc32(name.encode()), seed]).standard_normal(out[name].shape)
        drawn = base * np.exp(spread * noise) if base else spread * noise
        out[name] = jnp.asarray(drawn.astype(out[name].dtype))
    for name, factor in factors.items():
        out[name] = (out[name] * factor).astype(out[name].dtype)
    return out
```

```python
import numpy as np
import concourse.bass as bass
from concourse import mybir
from contextlib import ExitStack

F32 = mybir.dt.float32
BF16 = mybir.dt.bfloat16
I32 = mybir.dt.int32
ALU = mybir.AluOpType
ACT = mybir.ActivationFunctionType
AX = mybir.AxisListType

P = 128
SEQ = 2048
TILES = SEQ // P
HALF = 64
EPS = 1e-5

DEPTH = 6
HEADS = 16
DH = 64
WIN = 32
INNER = HEADS * DH
HP = HEADS // 2
FF = int(P * 4 * 2 / 3)
FCH = [(0, 128), (128, 128), (256, FF - 256)]
NCH = len(FCH)
PAIR = 2 * P
PAIRS = TILES // 2
MASKED = -1.0e38
NEWTON = 12

LK = 64
NS = 64
TWO_PI = 2 * np.pi
ROUND = 1.5 * 2 ** 23
TURN_HI = 6.28125
TURN_LO = TWO_PI - TURN_HI
SIN_MAX = 3.1415925
BLK = 32
NBLK = SEQ // BLK

BH = 16
BD = 8
CH = 512


def semaphore(nc, c, sems, name):
    sems.append(c.enter_context(nc.semaphore(name)))
    return sems[-1]


def clear(nc, sems):
    with nc.Block() as block:
        @block.sync
        def _(sp):
            for sm in sems:
                sp.sem_clear(sm)


class Shared:
    pass


def shifted(z, c0, n):
    return z[:, bass.ds(c0, n)]


def own(z, half, c0, n):
    if half == 0:
        return z[0:HALF, bass.ds(c0, n)]
    return z[HALF:P, bass.ds(c0 + 1, n)]


def load_phase(nc, g):
    sems = []
    with ExitStack() as c:
        arrived = semaphore(nc, c, sems, "consts_in")
        block_end = c.enter_context(ExitStack())
        block = block_end.enter_context(nc.Block())

        @block.sync
        def _(sp):
            sp.dma_start(g.x[:, :], g.d["x"]).then_inc(arrived, 16)
            sp.dma_start(g.ident[:, :], g.d["ident"]).then_inc(arrived, 16)
            sp.dma_start(g.identb[:, :], g.d["identb"]).then_inc(arrived, 16)
            sp.wait_ge(arrived, 48)

        @block.gpsimd
        def _(pool):
            nc.gpsimd.memset(g.mean_w[:, :], 1.0 / P)
            nc.gpsimd.memset(g.eps[:, :], EPS)
            nc.gpsimd.memset(g.zb[:, 0:1], 0.0)

        block_end.close()
        clear(nc, sems)


def norm_phase(nc, g, name, split):
    sems = []
    with ExitStack() as c:
        xc = c.enter_context(nc.sbuf_tensor(name + "_xc", [P, 4, CH], F32))
        sq = c.enter_context(nc.sbuf_tensor(name + "_sq", [P, 4, CH], F32))
        sd = c.enter_context(nc.sbuf_tensor(name + "_sd", [P, 4, CH], F32))
        rs = c.enter_context(nc.sbuf_tensor(name + "_rs", [P, 4, CH], F32))
        ps = c.enter_context(nc.psum_tensor(name + "_ps", [P, 8, CH], F32))
        s_mean = semaphore(nc, c, sems, name + "_mean")
        s_xc = semaphore(nc, c, sems, name + "_centred")
        s_sq = semaphore(nc, c, sems, name + "_squared")
        s_var = semaphore(nc, c, sems, name + "_var")
        s_sd = semaphore(nc, c, sems, name + "_sdev")
        s_rs = semaphore(nc, c, sems, name + "_rstd")
        block_end = c.enter_context(ExitStack())
        block = block_end.enter_context(nc.Block())

        @block.tensor
        def _(pe):
            for b in range(4):
                nc.tensor.matmul(ps[:, b, :], g.mean_w[:, :], g.x[:, CH * b:CH * b + CH],
                                 start=True, stop=True).then_inc(s_mean, 1)
            for b in range(4):
                pe.wait_ge(s_sq, b + 1)
                nc.tensor.matmul(ps[:, 4 + b, :], g.mean_w[:, :], sq[:, b, :],
                                 start=True, stop=True).then_inc(s_var, 1)

        @block.scalar
        def _(act):
            for b in range(4):
                act.wait_ge(s_xc, b + 1)
                nc.scalar.activation(sq[:, b, :], xc[:, b, :], ACT.Square).then_inc(s_sq, 1)
            for b in range(4):
                act.wait_ge(s_var, b + 1)
                nc.scalar.activation(sd[:, b, :], ps[:, 4 + b, :], ACT.Sqrt, bias=g.eps[:, 0:1]).then_inc(s_sd, 1)

        @block.vector
        def _(dve):
            if split:
                nc.vector.memset(g.za[HALF:P, 0:1], 0.0)
            for b in range(4):
                dve.wait_ge(s_mean, b + 1)
                nc.vector.tensor_tensor(xc[:, b, :], g.x[:, CH * b:CH * b + CH], ps[:, b, :],
                                        ALU.subtract).then_inc(s_xc, 1)
            for b in range(4):
                dve.wait_ge(s_sd, b + 1)
                nc.vector.reciprocal(rs[:, b, :], sd[:, b, :]).then_inc(s_rs, 1)
                dve.wait_ge(s_rs, b + 1)
                if split:
                    for h in range(2):
                        rows = slice(h * HALF, h * HALF + HALF)
                        nc.vector.tensor_tensor(own(g.za, h, CH * b, CH), xc[rows, b, :], rs[rows, b, :], ALU.mult)
                else:
                    nc.vector.tensor_tensor(g.za[:, CH * b:CH * b + CH], xc[:, b, :], rs[:, b, :], ALU.mult)

        block_end.close()
        clear(nc, sems)



def stack_phase(nc, g, name):
    sems = []
    with ExitStack() as c:
        def sb(n, shape, dt=F32):
            return c.enter_context(nc.sbuf_tensor(name + "_" + n, shape, dt))

        def sem(n):
            return semaphore(nc, c, sems, name + "_" + n)

        st_qkv = sb("st_qkv", [P, 3 * INNER])
        w_qkv = sb("w_qkv", [P, 3 * INNER])
        st_o = sb("st_o", [P, HP, P])
        w_o = sb("w_o", [P, HP, P])
        st_1 = sb("st_1", [P, 2 * FF])
        w_1 = sb("w_1", [P, 2 * FF])
        st_2 = sb("st_2", [P, NCH, P])
        w_2 = sb("w_2", [P, NCH, P])
        rope = sb("rope", [P, TILES, 4, DH])
        qks = sb("qks", [P, DEPTH, 4, DH])
        b1c = sb("b1c", [P, DEPTH, 2, NCH])
        b2c = sb("b2c", [P, DEPTH])
        w_b1 = sb("w_b1", [P, 2, NCH])
        w_b2 = sb("w_b2", [P, 1])
        lng = sb("lng", [P, DEPTH])
        lnb = sb("lnb", [P, DEPTH])
        mask = sb("mask", [P, 2, P], BF16)
        carry_w = sb("carry_w", [P, 1])
        xst = sb("xst", [P, 2, P])
        tab = sb("tab", [P, 2, 4, DH])
        sq = sb("sq", [P, 2, INNER])
        rot1 = sb("rot1", [P, 2, INNER])
        rot2 = sb("rot2", [P, 2, INNER])
        n2 = sb("n2", [P, 2 * HEADS])
        nx = sb("nx", [P, 2 * HEADS])
        ny = sb("ny", [P, 2 * HEADS])
        nt = sb("nt", [P, 2 * HEADS])
        qn = sb("qn", [P, 2, INNER])
        kn = sb("kn", [P, 2, INNER])
        qT = sb("qT", [P, HP, 4, 2, WIN])
        kT = sb("kT", [P, 2, HP, WIN + P])
        smax = sb("smax", [P, HEADS])
        ssum = sb("ssum", [P, HEADS])
        sinv = sb("sinv", [P, HEADS])
        prob = sb("prob", [P, 2, INNER])
        aT = sb("aT", [P, HP, 2, 2, 2, WIN])
        vA = sb("vA", [P, 2, INNER])
        vB = sb("vB", [P, 2, INNER])
        oT = sb("oT", [P, HP, P])
        xc = sb("xc", [P, PAIR])
        xq = sb("xq", [P, PAIR])
        xd = sb("xd", [P, PAIR])
        xr = sb("xr", [P, PAIR])
        xm = sb("xm", [P, PAIR])
        xn = sb("xn", [P, PAIR])
        gel = sb("gel", [P, NCH, PAIR])
        hT = sb("hT", [P, NCH, PAIR])
        ps = [c.enter_context(nc.psum_tensor(f"{name}_ps{i}", [P, 2 * CH], F32)) for i in range(4)]

        consts = sem("consts")
        zeroed = sem("zeroed")
        qkv_staged, o_staged, ff_staged = sem("qkv_staged"), sem("o_staged"), sem("ff_staged")
        qkv_set, o_set, ff_set = sem("qkv_set"), sem("o_set"), sem("ff_set")
        q_mm, k_mm, v_mm = sem("q_mm"), sem("k_mm"), sem("v_mm")
        qT_mm, kT_mm, aT_mm = sem("qT_mm"), sem("kT_mm"), sem("aT_mm")
        s_mm, oA_mm, o_mm, y_mm = sem("s_mm"), sem("oA_mm"), sem("o_mm"), sem("y_mm")
        q_sq, k_sq, v_sb = sem("q_sq"), sem("k_sq"), sem("v_sb")
        qT_sb, kT_sb, aT_sb, oT_sb = sem("qT_sb"), sem("kT_sb"), sem("aT_sb"), sem("oT_sb")
        exp_done = sem("exp_done")
        x_st, q_rot, k_rot = sem("x_st"), sem("q_rot"), sem("k_rot")
        q_n2, k_n2, newton = sem("q_n2"), sem("k_n2"), sem("newton")
        q_n, k_n = sem("q_n"), sem("k_n")
        max_done, sub_done, sum_done, inv_done = sem("max_done"), sem("sub_done"), sem("sum_done"), sem("inv_done")
        zb_done = sem("zb_done")
        tab_done, carry_done, q_add, k_add, a_done = (sem("tab_done"), sem("carry_done"), sem("q_add"),
                                                      sem("k_add"), sem("a_done"))
        vB_dma = sem("vB_dma")
        mean_mm, var_mm, hg_mm, ha_mm, y2_mm = (sem("mean_mm"), sem("var_mm"), sem("hg_mm"), sem("ha_mm"),
                                                sem("y2_mm"))
        xc_done, xq_done, xd_done = sem("xc_done"), sem("xq_done"), sem("xd_done")
        xr_done, xm_done, xn_done = sem("xr_done"), sem("xm_done"), sem("xn_done")
        gel_done, h_done, za_done = sem("gel_done"), sem("h_done"), sem("za_done")

        block_end = c.enter_context(ExitStack())
        block = block_end.enter_context(nc.Block())

        def wait(eng, sm, value):
            if not isinstance(value, int) or value > 0:
                eng.wait_ge(sm, value)

        CONSTS = 16 * 8


        def walk(eng, pair, switch):
            on, off = (True, True), (False, False)
            every = dict(S1=True, S2=on, S3=on, S4=on, FS=True, FP=True)
            switch(0, 0)
            pair(L=0, p=0, G=0, S1=True, S2=(False, True), S3=off, S4=off, FS=False, FP=False)
            pair(L=0, p=1, G=1, new_o=True, S1=True, S2=on, S3=on, S4=(False, True), FS=False, FP=False)
            pair(L=0, p=2, G=2, S1=True, S2=on, S3=on, S4=on, FS=True, FP=False)
            switch(2, 0)
            pair(L=0, p=3, G=3, **every)
            with eng.Fori(0, DEPTH - 1) as L:
                with eng.Fori(4, PAIRS) as p:
                    pair(L=L, p=p, G=L * PAIRS + p, **every)
                switch(0, L + 1)
                pair(L=L + 1, p=0, G=L * PAIRS + PAIRS, **every)
                pair(L=L + 1, p=1, G=L * PAIRS + PAIRS + 1, new_o=True, **every)
                pair(L=L + 1, p=2, G=L * PAIRS + PAIRS + 2, **every)
                switch(2, L + 1)
                pair(L=L + 1, p=3, G=L * PAIRS + PAIRS + 3, **every)
            L = DEPTH - 1
            with eng.Fori(4, PAIRS) as p:
                pair(L=L, p=p, G=L * PAIRS + p, **every)
            pair(L=DEPTH, p=0, G=DEPTH * PAIRS, S1=False, S2=(True, False), S3=on, S4=on, FS=True, FP=True)
            pair(L=DEPTH, p=1, G=DEPTH * PAIRS + 1, S1=False, S2=off, S3=off, S4=(True, False), FS=True, FP=True)
            pair(L=DEPTH, p=2, G=DEPTH * PAIRS + 2, S1=False, S2=off, S3=off, S4=off, FS=False, FP=True)

        def heads(ap):
            return ap.rearrange("p (h d) -> p h d", d=DH)

        def each_head(ap):
            return ap.rearrange("p (h a) -> p h a", a=1).to_broadcast([P, HEADS, DH])

        def back(L, p, n):
            if isinstance(p, int) and p < n:
                return L - 1, PAIRS + p - n
            return L, p - n

        def load_qkv(eng, L):
            eng.dma_start(st_qkv[:, :], g.d["Wqkv"][bass.ds(L, 1), :, :].rearrange("a p n -> p (a n)")
                         ).then_inc(qkv_staged, 16)

        def load_o(eng, L):
            eng.dma_start(st_o[:, :, :], g.d["Wo"][bass.ds(L, 1), :, :].rearrange("a (c p) n -> p (a c) n", p=P)
                         ).then_inc(o_staged, 16)

        def load_ff(eng, L):
            eng.dma_start(st_1[:, :], g.d["W1"][bass.ds(L, 1), :, :].rearrange("a p n -> p (a n)")
                         ).then_inc(ff_staged, 16)
            eng.dma_start(st_2[:, 0:2, :],
                         g.d["W2"][bass.ds(L, 1), 0:2 * P, :].rearrange("a (c p) n -> p (a c) n", p=P)
                         ).then_inc(ff_staged, 16)
            eng.dma_start(st_2[0:FF - 2 * P, 2, :],
                         g.d["W2"][bass.ds(L, 1), 2 * P:FF, :].rearrange("a p n -> p (a n)")
                         ).then_inc(ff_staged, 16)

        def after(L):
            return (L + 1) % DEPTH

        @block.sync
        def _(sp):
            n = 0
            for dst, src in ((rope[:, :, :, :], g.d["rope"].rearrange("p (t f d) -> p t f d", t=TILES, f=4)),
                             (mask[:, :, :], g.d["mask"].rearrange("p (a b) -> p a b", a=2)),
                             (carry_w[:, :], g.d["carry"]),
                             (b2c[:, :], g.d["b2"]), (lng[:, :], g.d["ln_g"]), (lnb[:, :], g.d["ln_b"]),
                             (b1c[:, :, :, :], g.d["b1"].rearrange("p (l a b) -> p l a b", l=DEPTH, a=2)),
                             (qks[:, :, :, :], g.d["qk_scale"].partition_broadcast(P))):
                sp.dma_start(dst, src).then_inc(consts, 16)
                n += 16
            assert n == CONSTS

            load_qkv(sp, 0)
            load_o(sp, 0)
            load_ff(sp, 0)
            sp.wait_ge(zeroed, 3)

            def pair(L, p, G, S1, S2, S3, S4, FS, FP, new_o=False):
                if not S1:
                    return
                for e in range(2):
                    T = G * 2 + e
                    if e == 1 and S3[e]:
                        sp.wait_ge(oT_sb, T - 1)
                    else:
                        sp.wait_ge(v_sb, T + 1)
                    sp.dma_start(vB[WIN:P, e, :], vA[0:P - WIN, e, :]).then_inc(vB_dma, 16)
                    sp.dma_start(vB[0:WIN, e, :], vA[P - WIN:P, 1 - e, :]).then_inc(vB_dma, 16)

            walk(sp, pair, lambda which, L: None)
            sp.wait_ge(vB_dma, 32 * DEPTH * TILES)
            sp.wait_ge(qkv_staged, 16 * (DEPTH + 1))
            sp.wait_ge(o_staged, 16 * (DEPTH + 1))
            sp.wait_ge(ff_staged, 48 * (DEPTH + 1))


        @block.tensor
        def _(pe):
            pe.wait_ge(consts, CONSTS)
            pe.wait_ge(zeroed, 3)

            def pair(L, p, G, S1, S2, S3, S4, FS, FP, new_o=False):
                for e in range(2):
                    if new_o and e == 1:
                        switch(1, L)
                    tile_step(L, p, G, e, S1, S2[e], S3[e], S4[e], FS, FP)

            def key_product(T, G, e, S1, FS, FP):
                if S1:
                    if e == 0:
                        if FS:
                            wait(pe, xd_done, G - 2)
                        if FP:
                            wait(pe, za_done, G - 3)
                    else:
                        if FS:
                            wait(pe, xc_done, G - 1)
                        if FP:
                            wait(pe, h_done, G - 2)
                    for j in range(2):
                        mm = nc.tensor.matmul(ps[1][:, j * CH:j * CH + CH], xst[:, e, :],
                                              w_qkv[:, INNER + j * CH:INNER + j * CH + CH], start=True, stop=True)
                    mm.then_inc(k_mm, 1)

            def projection(T, G, e, S4, FP):
                if S4:
                    pe.wait_ge(oT_sb, T - 2)
                    if FP and e == 1:
                        wait(pe, gel_done, G - 2)
                    for hp in range(HP):
                        mm = nc.tensor.matmul(ps[2][:, 0:P], w_o[:, hp, :], oT[:, hp, :],
                                              start=(hp == 0), stop=(hp == HP - 1))
                    mm.then_inc(y_mm, 1)

            def tile_step(L, p, G, e, S1, S2, S3, S4, FS, FP):
                T = G * 2 + e
                first = isinstance(p, int) and p == 0 and e == 1
                if S1:
                    pe.wait_ge(x_st, T + 1)
                    wait(pe, v_sb, T)
                    for j in range(2):
                        mm = nc.tensor.matmul(ps[3][:, j * CH:j * CH + CH], xst[:, e, :],
                                              w_qkv[:, j * CH:j * CH + CH], start=True, stop=True)
                    mm.then_inc(q_mm, 1)
                if S2:
                    pe.wait_ge(q_n, T)
                    wait(pe, sub_done, T - 1)
                    for j in range(HP):
                        mm = nc.tensor.transpose(ps[0][:, j * P:j * P + P], qn[:, 1 - e, j * P:j * P + P],
                                                 g.ident[:, :])
                    mm.then_inc(qT_mm, 1)
                if e == 0:
                    key_product(T, G, e, S1, FS, FP)
                else:
                    projection(T, G, e, S4, FP)
                    key_product(T, G, e, S1, FS, FP)
                if S2:
                    pe.wait_ge(k_n, T)
                    pe.wait_ge(qT_sb, T)
                    for j in range(HP):
                        mm = nc.tensor.transpose(ps[0][:, j * P:j * P + P], kn[:, 1 - e, j * P:j * P + P],
                                                 g.ident[:, :])
                    mm.then_inc(kT_mm, 1)
                if e == 0:
                    projection(T, G, e, S4, FP)
                if S2:
                    pe.wait_ge(kT_sb, T)
                    pe.wait_ge(carry_done, T)
                    for b in range(2):
                        m = mask[:, 1 if first else 0, :].rearrange("p (a n) -> p a n", a=1)
                        nc.tensor.matmul(ps[0][:, b * CH:b * CH + CH].rearrange("p (h n) -> p h n", n=P),
                                         g.identb[:, :], m.to_broadcast([P, 4, P]),
                                         start=True, stop=False, skip_group_check=True)
                        for u in range(2):
                            for hp in range(4 * b, 4 * b + 4):
                                for wg in range(2):
                                    w = 2 * wg + u
                                    mm = nc.tensor.matmul(
                                        ps[0][64 * u:64 * u + 64, hp * P + wg * 64:hp * P + wg * 64 + 64],
                                        qT[:, hp, w, :, :].rearrange("p a b -> p (a b)"),
                                        kT[:, 1 - e, hp, WIN * w:WIN * w + 2 * WIN],
                                        start=False, stop=(u == 1), skip_group_check=True)
                    mm.then_inc(s_mm, 1)
                if S3:
                    pe.wait_ge(a_done, T - 1)
                    if S4:
                        pe.wait_ge(zb_done, T - 2)
                    for j in range(HP):
                        mm = nc.tensor.transpose(ps[2][:, j * P:j * P + P], prob[:, e, j * P:j * P + P],
                                                 g.ident[:, :])
                    mm.then_inc(aT_mm, 1)
                if FS or FP and e == 1:
                    Lf, pf = back(L, p, 2)
                    if S1:
                        pe.wait_ge(k_sq, T + 1)
                        pe.wait_ge(k_rot, T + 1)
                    elif e == 0:
                        pe.wait_ge(za_done, G - 3)
                if FS and e == 0:
                    pe.wait_ge(zb_done, 2 * G - 2)
                    if not S1:
                        pe.wait_ge(xd_done, G - 2)
                    nc.tensor.matmul(ps[1][:, 0:PAIR], g.mean_w[:, :], shifted(g.zb, pf * PAIR, PAIR),
                                     start=True, stop=True).then_inc(mean_mm, 1)
                if FS and e == 1:
                    pe.wait_ge(xq_done, G - 1)
                    if FP and not S1:
                        pe.wait_ge(h_done, G - 2)
                    nc.tensor.matmul(ps[1][:, 0:PAIR], g.mean_w[:, :], xq[:, :],
                                     start=True, stop=True).then_inc(var_mm, 1)
                if FP and e == 1:
                    pe.wait_ge(h_done, G - 2)
                    for j, (f0, fn) in enumerate(FCH):
                        mm = nc.tensor.matmul(ps[1][:, CH:CH + PAIR], w_2[0:fn, j, :], hT[0:fn, j, :],
                                              start=(j == 0), stop=(j == NCH - 1))
                    mm.then_inc(y2_mm, 1)
                if S1:
                    pe.wait_ge(q_sq, T + 1)
                    pe.wait_ge(q_rot, T + 1)
                    for j in range(2):
                        mm = nc.tensor.matmul(ps[3][:, j * CH:j * CH + CH], xst[:, e, :],
                                              w_qkv[:, 2 * INNER + j * CH:2 * INNER + j * CH + CH],
                                              start=True, stop=True)
                    mm.then_inc(v_mm, 1)
                if S3:
                    pe.wait_ge(aT_sb, T - 1)
                    for u, through in ((1, oA_mm), (0, o_mm)):
                        v = vA if u else vB
                        if u == 0:
                            pe.wait_ge(vB_dma, 32 * (T - 1))
                        for h2 in range(2):
                            for hp in range(HP):
                                h = 2 * hp + h2
                                out = ps[2][64 * h2:64 * h2 + 64, hp * P:hp * P + P]
                                mm = nc.tensor.matmul(
                                    out.rearrange("p (a b i) -> p a b i", a=2, b=2)[:, :, u, :],
                                    v[:, e, h * DH:h * DH + DH],
                                    aT[:, hp, u, h2, :, :].rearrange("p a b -> p (a b)"),
                                    start=True, stop=True, skip_group_check=True)
                        mm.then_inc(through, 1)
                if FP and e == 0:
                    pe.wait_ge(xn_done, G - 2)
                    if FS:
                        pe.wait_ge(xc_done, G - 1)
                    elif not S1:
                        pe.wait_ge(za_done, G - 3)
                    for j, (f0, fn) in enumerate(FCH):
                        mm = nc.tensor.matmul(ps[1][0:fn, j * PAIR:(j + 1) * PAIR], w_1[:, f0:f0 + fn],
                                              xn[:, :], start=True, stop=True, skip_group_check=True)
                    mm.then_inc(ha_mm, 1)
                    if S3:
                        pe.wait_ge(oT_sb, T - 1)
                    else:
                        pe.wait_ge(gel_done, G - 3)
                        if S4:
                            pe.wait_ge(zb_done, T - 2)
                    for j, (f0, fn) in enumerate(FCH):
                        mm = nc.tensor.matmul(ps[2][0:fn, j * PAIR:j * PAIR + PAIR], w_1[:, FF + f0:FF + f0 + fn],
                                              xn[:, :], start=True, stop=True, skip_group_check=True)
                    mm.then_inc(hg_mm, 1)

            def switch(which, L):
                pe.wait_ge((qkv_set, o_set, ff_set)[which], L + 1)

            walk(pe, pair, switch)

        @block.scalar
        def _(act):
            act.wait_ge(consts, CONSTS)
            act.wait_ge(zeroed, 3)

            def pair(L, p, G, S1, S2, S3, S4, FS, FP, new_o=False):
                for e in range(2):
                    if new_o and e == 1:
                        switch(1, L)
                    tile_step(L, p, G, e, S1, S2[e], S3[e], FS, FP)

            def tile_step(L, p, G, e, S1, S2, S3, FS, FP):
                T = G * 2 + e
                if S2:
                    act.wait_ge(qT_mm, T)
                    wait(act, s_mm, T - 1)
                    for h2 in range(2):
                        r = slice(64 * h2, 64 * h2 + 64)
                        last = nc.scalar.activation(
                            qT[r, :, :, h2, :].rearrange("p a b c -> p (a b) c"),
                            ps[0][r, :].rearrange("p (a c) -> p a c", c=WIN), ACT.Copy)
                    last.then_inc(qT_sb, 1)
                if S1:
                    act.wait_ge(q_rot, T + 1)
                    wait(act, q_n2, T)
                    nc.scalar.activation(sq[:, 0, :], ps[3][:, :], ACT.Square).then_inc(q_sq, 1)
                if S2:
                    act.wait_ge(kT_mm, T)
                    wait(act, carry_done, T - 1)
                    nc.scalar.activation(kT[:, 1 - e, :, WIN:WIN + P],
                                         ps[0][:, :].rearrange("p (a c) -> p a c", c=P), ACT.Copy).then_inc(kT_sb, 1)
                if S1:
                    act.wait_ge(k_rot, T + 1)
                    wait(act, k_n2, T)
                    nc.scalar.activation(sq[:, 1, :], ps[1][:, :], ACT.Square).then_inc(k_sq, 1)
                if S3:
                    act.wait_ge(aT_mm, T - 1)
                    wait(act, o_mm, T - 2)
                    for wg in range(2):
                        r = slice(64 * wg, 64 * wg + 64)
                        last = nc.scalar.activation(
                            aT[r, :, :, :, wg, :].rearrange("p a b c d -> p (a b c) d"),
                            ps[2][r, :].rearrange("p (a c) -> p a c", c=WIN), ACT.Copy)
                    last.then_inc(aT_sb, 1)
                if FS and e == 1:
                    act.wait_ge(var_mm, G - 1)
                    wait(act, xr_done, G - 2)
                    nc.scalar.activation(xd[:, :], ps[1][:, 0:PAIR], ACT.Sqrt, bias=g.eps[:, 0:1]
                                         ).then_inc(xd_done, 1)
                for part in (("output", "values") if e == 0 else ("values", "output")):
                    if part == "output" and S3:
                        act.wait_ge(o_mm, T - 1)
                        wait(act, y_mm, T - 2)
                        nc.scalar.activation(oT[:, :, :].rearrange("p a b -> p (a b)"), ps[2][:, :], ACT.Copy
                                             ).then_inc(oT_sb, 1)
                    if part == "values" and S1:
                        act.wait_ge(v_mm, T + 1)
                        wait(act, oA_mm, T - 1)
                        wait(act, vB_dma, 32 * T)
                        nc.scalar.activation(vA[:, e, :], ps[3][:, :], ACT.Copy).then_inc(v_sb, 1)
                if S2:
                    act.wait_ge(sub_done, T)
                    nc.scalar.activation(prob[:, 1 - e, :], prob[:, 1 - e, :], ACT.Exp).then_inc(exp_done, 1)
                if FS and e == 0:
                    act.wait_ge(xc_done, G - 1)
                    wait(act, var_mm, G - 2)
                    nc.scalar.activation(xq[:, :], xc[:, :], ACT.Square).then_inc(xq_done, 1)
                if FP and e == 0:
                    act.wait_ge(hg_mm, G - 2)
                    wait(act, h_done, G - 3)
                    for j, (f0, fn) in enumerate(FCH):
                        last = nc.scalar.activation(gel[0:fn, j, :], ps[2][0:fn, j * PAIR:j * PAIR + PAIR], ACT.Gelu,
                                                    bias=w_b1[0:fn, 1, j:j + 1])
                    last.then_inc(gel_done, 1)

            def switch(which, L):
                if which == 1:
                    act.wait_ge(qkv_set, L + 1)
                    load_qkv(act, after(L))
                if which == 2:
                    act.wait_ge(o_set, L + 1)
                    load_o(act, after(L))
                    act.wait_ge(ff_set, L + 1)
                    load_ff(act, after(L))

            walk(act, pair, switch)

        @block.vector
        def _(dve):
            dve.wait_ge(consts, CONSTS)
            dve.wait_ge(zeroed, 3)

            def pair(L, p, G, S1, S2, S3, S4, FS, FP, new_o=False):
                for e in range(2):
                    if new_o and e == 1:
                        switch(1, L)
                    tile_step(L, p, G, e, S1, S2[e], S3[e], S4[e], FS, FP)

            def rotate(x, slot, T, e, done):
                src = ps[slot][:, :].rearrange("p (h d) -> p h d", d=DH)
                cos = tab[:, e, 2 * x, :].rearrange("p (a d) -> p a d", a=1)
                nc.vector.tensor_tensor(rot1[:, x, :].rearrange("p (h d) -> p h d", d=DH), src,
                                        cos.to_broadcast([P, HEADS, DH]), ALU.mult)
                half = DH // 2
                swapped = ps[slot][:, :].rearrange("p (h a d) -> p h a d", a=2, d=half)[:, :, ::-1, :]
                sin = tab[:, e, 2 * x + 1, :].rearrange("p (o a d) -> p o a d", o=1, a=2)
                nc.vector.tensor_tensor(rot2[:, x, :].rearrange("p (h a d) -> p h a d", a=2, d=half), swapped,
                                        sin.to_broadcast([P, HEADS, 2, half]), ALU.mult).then_inc(done, 1)

            def rsqrt(T):
                v = nc.vector
                n = [0]

                def link(ins):
                    n[0] += 1
                    ins.then_inc(newton, 1)
                    dve.wait_ge(newton, T * NEWTON + n[0])

                link(v.tensor_scalar(nx[:, :], n2[:, :], 1e-24, None, ALU.max))
                link(v.tensor_scalar(nt[:, :].bitcast(I32), nx[:, :].bitcast(I32), 1, None, ALU.logical_shift_right))
                link(v.tensor_scalar(ny[:, :].bitcast(I32), nt[:, :].bitcast(I32), -1.0, float(0x5f3759df),
                                     ALU.mult, ALU.add))
                for _ in range(3):
                    link(v.tensor_tensor(nt[:, :], ny[:, :], ny[:, :], ALU.mult))
                    link(v.scalar_tensor_tensor(nt[:, :], nt[:, :], -0.5, nx[:, :], ALU.mult, ALU.mult))
                    link(v.scalar_tensor_tensor(ny[:, :], nt[:, :], 1.5, ny[:, :], ALU.add, ALU.mult))

            def tile_step(L, p, G, e, S1, S2, S3, S4, FS, FP):
                T = G * 2 + e
                if S1:
                    wait(dve, v_mm, T - 1)
                    nc.vector.tensor_copy(xst[:, e, :], shifted(g.za, p * PAIR + e * P, P)).then_inc(x_st, 1)
                if FP and e == 0:
                    Lf, pf = back(L, p, 3)
                    dve.wait_ge(xd_done, G - 2)
                    nc.vector.reciprocal(xr[:, :], xd[:, :]).then_inc(xr_done, 1)
                    dve.wait_ge(xr_done, G - 2)
                    nc.vector.tensor_tensor(xm[:, :], xc[:, :], xr[:, :], ALU.mult).then_inc(xm_done, 1)
                    dve.wait_ge(xm_done, G - 2)
                    wait(dve, hg_mm, G - 3)
                    nc.vector.tensor_scalar(xn[:, :], xm[:, :], col(lng, Lf, 1, 0), col(lnb, Lf, 1, 0),
                                            ALU.mult, ALU.add).then_inc(xn_done, 1)
                if S1:
                    dve.wait_ge(q_mm, T + 1)
                    dve.wait_ge(tab_done, T + 1)
                    wait(dve, q_n, T)
                    rotate(0, 3, T, e, q_rot)
                if FP and e == 1:
                    dve.wait_ge(ha_mm, G - 2)
                    dve.wait_ge(gel_done, G - 2)
                    wait(dve, y2_mm, G - 3)
                    for j, (f0, fn) in enumerate(FCH):
                        last = nc.vector.scalar_tensor_tensor(hT[0:fn, j, :],
                                                              ps[1][0:fn, j * PAIR:(j + 1) * PAIR],
                                                              w_b1[0:fn, 0, j:j + 1], gel[0:fn, j, :],
                                                              ALU.add, ALU.mult)
                    last.then_inc(h_done, 1)
                if S3:
                    dve.wait_ge(exp_done, T - 1)
                    nc.vector.tensor_reduce(ssum[:, :], heads(prob[:, e, :]), AX.X, ALU.add).then_inc(sum_done, 1)
                    dve.wait_ge(sum_done, T - 1)
                    wait(dve, a_done, T - 2)
                    nc.vector.reciprocal(sinv[:, :], ssum[:, :]).then_inc(inv_done, 1)
                if S1:
                    dve.wait_ge(k_mm, T + 1)
                    wait(dve, k_n, T)
                    rotate(1, 1, T, e, k_rot)
                if S4:
                    Ls, pt = back(L, p, 2 - e)
                    dve.wait_ge(y_mm, T - 2)
                    for h in range(2):
                        last = nc.vector.tensor_tensor(own(g.zb, h, pt * PAIR + (1 - e) * P, P),
                                                       own(g.za, h, pt * PAIR + (1 - e) * P, P),
                                                       ps[2][h * HALF:h * HALF + HALF, 0:P], ALU.add)
                    last.then_inc(zb_done, 1)
                if S1:
                    dve.wait_ge(q_sq, T + 1)
                    nc.vector.tensor_reduce(n2[:, 0:HEADS], heads(sq[:, 0, :]), AX.X, ALU.add).then_inc(q_n2, 1)
                    dve.wait_ge(k_sq, T + 1)
                    nc.vector.tensor_reduce(n2[:, HEADS:2 * HEADS], heads(sq[:, 1, :]), AX.X, ALU.add
                                            ).then_inc(k_n2, 1)
                if S2:
                    dve.wait_ge(s_mm, T)
                    nc.vector.tensor_reduce(smax[:, :], heads(ps[0][:, :]), AX.X, ALU.max).then_inc(max_done, 1)
                    dve.wait_ge(max_done, T)
                    wait(dve, aT_mm, T - 2)
                    nc.vector.tensor_tensor(heads(prob[:, 1 - e, :]), heads(ps[0][:, :]), each_head(smax[:, :]),
                                            ALU.subtract).then_inc(sub_done, 1)
                if FS and e == 0:
                    Lf, pf = back(L, p, 2)
                    dve.wait_ge(mean_mm, G - 1)
                    wait(dve, xm_done, G - 2)
                    nc.vector.tensor_tensor(xc[:, :], shifted(g.zb, pf * PAIR, PAIR), ps[1][:, 0:PAIR],
                                            ALU.subtract).then_inc(xc_done, 1)
                if S1:
                    dve.wait_ge(k_n2, T + 1)
                    rsqrt(T)
                    wait(dve, qT_mm, T - 1)
                    dve.wait_ge(q_add, T + 1)
                    nc.vector.tensor_tensor(heads(qn[:, e, :]), heads(rot1[:, 0, :]), each_head(ny[:, 0:HEADS]),
                                            ALU.mult).then_inc(q_n, 1)
                if FP and e == 1:
                    Lf, pf = back(L, p, 3)
                    dve.wait_ge(y2_mm, G - 2)
                    for h in range(2):
                        r = slice(h * HALF, h * HALF + HALF)
                        last = nc.vector.scalar_tensor_tensor(own(g.za, h, pf * PAIR, PAIR), ps[1][r, CH:CH + PAIR],
                                                              w_b2[r, :],
                                                              own(g.zb, h, pf * PAIR, PAIR), ALU.add, ALU.add)
                    last.then_inc(za_done, 1)

            def switch(which, L):
                if which == 0:
                    dve.wait_ge(qkv_staged, 16 * (L + 1))
                    wait(dve, v_mm, L * TILES)
                    nc.vector.tensor_copy(w_qkv[:, :], st_qkv[:, :]).then_inc(qkv_set, 1)
                elif which == 1:
                    dve.wait_ge(o_staged, 16 * (L + 1))
                    wait(dve, y_mm, L * TILES)
                    nc.vector.tensor_copy(w_o[:, :, :], st_o[:, :, :]).then_inc(o_set, 1)
                else:
                    dve.wait_ge(ff_staged, 48 * (L + 1))
                    wait(dve, y2_mm, L * PAIRS)
                    wait(dve, za_done, L * PAIRS)
                    nc.vector.tensor_copy(w_b1[:, :, :].rearrange("p a b -> p (a b)"), col(b1c, L, 2 * NCH, 0, 2 * NCH))
                    nc.vector.tensor_copy(w_b2[:, :], col(b2c, L, 1, 0))
                    nc.vector.tensor_copy(w_1[:, :], st_1[:, :])
                    nc.vector.tensor_copy(w_2[:, 0:2, :], st_2[:, 0:2, :])
                    nc.vector.tensor_copy(w_2[0:FF - 2 * P, 2, :], st_2[0:FF - 2 * P, 2, :]).then_inc(ff_set, 1)

            walk(dve, pair, switch)
            dve.wait_ge(za_done, DEPTH * PAIRS)
            for h in range(2):
                r = slice(h * HALF, h * HALF + HALF)
                nc.vector.tensor_tensor(g.x[r, :], g.x[r, :], own(g.za, h, 0, SEQ), ALU.add)

        @block.gpsimd
        def _(pool):
            nc.gpsimd.memset(qT[:, :, :, :, :], 0.0)
            nc.gpsimd.memset(aT[:, :, :, :, :, :], 0.0).then_inc(zeroed, 1)
            nc.gpsimd.memset(kT[:, 1, :, :], 0.0).then_inc(zeroed, 1)
            nc.gpsimd.memset(vA[:, 1, :], 0.0).then_inc(zeroed, 1)
            pool.wait_ge(zeroed, 3)
            pool.wait_ge(consts, CONSTS)

            def pair(L, p, G, S1, S2, S3, S4, FS, FP, new_o=False):
                for e in range(2):
                    tile_step(L, p, G, e, S1, S2[e], S3[e])

            def tile_step(L, p, G, e, S1, S2, S3):
                T = G * 2 + e
                if S1:
                    nc.gpsimd.tensor_tensor(
                        tab[:, e, :, :].rearrange("p f d -> p (f d)"),
                        col(rope, p * 2 + e, 4 * DH, 0, 4 * DH), col(qks, L, 4 * DH, 0, 4 * DH),
                        ALU.mult).then_inc(tab_done, 1)
                if S2:
                    wait(pool, kT_sb, T - 1)
                    wait(pool, s_mm, T - 2)
                    wait(pool, k_rot, T - 1)
                    nc.gpsimd.tensor_tensor(kT[:, 1 - e, :, 0:WIN], kT[:, e, :, P:P + WIN],
                                            carry_w[:, :].rearrange("p (a b) -> p a b", b=1).to_broadcast(
                                                [P, HP, WIN]), ALU.mult).then_inc(carry_done, 1)
                if S1:
                    pool.wait_ge(q_rot, T + 1)
                    nc.gpsimd.tensor_tensor(rot1[:, 0, :], rot1[:, 0, :], rot2[:, 0, :], ALU.add).then_inc(q_add, 1)
                if S3:
                    pool.wait_ge(inv_done, T - 1)
                    nc.gpsimd.tensor_tensor(heads(prob[:, e, :]), heads(prob[:, e, :]), each_head(sinv[:, :]),
                                            ALU.mult).then_inc(a_done, 1)
                if S1:
                    pool.wait_ge(k_rot, T + 1)
                    nc.gpsimd.tensor_tensor(rot1[:, 1, :], rot1[:, 1, :], rot2[:, 1, :], ALU.add).then_inc(k_add, 1)
                    pool.wait_ge(newton, NEWTON * (T + 1))
                    pool.wait_ge(k_add, T + 1)
                    wait(pool, kT_mm, T - 1)
                    nc.gpsimd.tensor_tensor(heads(kn[:, e, :]), heads(rot1[:, 1, :]),
                                            each_head(ny[:, HEADS:2 * HEADS]), ALU.mult).then_inc(k_n, 1)
            walk(pool, pair, lambda which, L: None)

        block_end.close()
        clear(nc, sems)


def col(buf, index, stride, off, n=1):
    names = "abcd"[:len(buf.shape) - 1]
    flat = buf[tuple([slice(None)] * len(buf.shape))]
    if len(names) > 1:
        flat = flat.rearrange("p %s -> p (%s)" % (" ".join(names), " ".join(names)))
    return flat[:, bass.ds(index * stride + off, n)]


def conv_phase(nc, g):
    sems = []
    with ExitStack() as c:
        def sb(n, shape, dt=F32):
            return c.enter_context(nc.sbuf_tensor("cv_" + n, shape, dt))

        def sem(n):
            return semaphore(nc, c, sems, "cv_" + n)

        prm = sb("prm", [P, 2 * NS])
        lam = sb("lam", [P, 2 * NS])
        cold = sb("cold", [P, 2])
        steps = sb("steps", [P, 2, 8, NS])
        dt_ = sb("dt", [P, 1])
        elr = sb("elr", [P, NS])
        ab = sb("ab", [P, 2, NS])
        ea = sb("ea", [P, 2, 8, NS])
        th = sb("th", [P, 2, 8, NS])
        turns = sb("turns", [P, 2, 2 * 8 * NS])
        ang = sb("ang", [P, 2, 2 * 8 * NS])
        sc = sb("sc", [P, 2, 2 * 8 * NS])
        mag = sb("mag", [P, 2 * 8 * NS])
        z = sb("z", [P, 2, 2, 8, NS])
        u = sb("u", [P, 4, 8, NS])
        uw = sb("uw", [P, 2, 8, NS])
        prod = sb("prod", [P, 8, 8 * NS])
        prod2 = sb("prod2", [P, 8, 8 * NS])
        taps = sb("taps", [P, LK])
        pad = sb("pad", [P, P])
        toep = sb("toep", [P, BLK, 3, 4, BLK])
        ut = sb("ut", [P, NBLK + 2, BLK])
        y = sb("y", [P, NBLK, BLK])
        yT = sb("yT", [P, SEQ])
        ps = c.enter_context(nc.psum_tensor("cv_ps", [P, 4, CH], F32))
        kd = nc.dram_tensor("taps_scratch", [P, P], F32, kind="Internal").ap()
        loaded, exps, chain = sem("loaded"), sem("exps"), sem("chain")
        args_done, trig_done, pad_done = sem("args_done"), sem("trig_done"), sem("pad_done")
        pad_stored, toep_zero, toep_in = sem("pad_stored"), sem("toep_zero"), sem("toep_in")
        ut_done, conv_mm, y_done = sem("ut_done"), sem("conv_mm"), sem("y_done")
        block_end = c.enter_context(ExitStack())
        block = block_end.enter_context(nc.Block())

        @block.sync
        def _(sp):
            for dst, src in ((prm[:, :], g.d["W_ri"]), (lam[:, :], g.d["lam"].partition_broadcast(P)),
                             (cold[:, :], g.d["dt_D"]),
                             (steps[:, :, :, :].rearrange("p a b n -> p (a b n)"),
                              g.d["steps"].partition_broadcast(P))):
                sp.dma_start(dst, src).then_inc(loaded, 16)
            sp.wait_ge(pad_done, 1)
            sp.dma_start(kd, pad[:, :]).then_inc(pad_stored, 16)
            sp.wait_ge(pad_stored, 16)
            sp.wait_ge(toep_zero, 1)
            for q in range(4):
                for b in range(3):
                    src = bass.AP(tensor=kd.tensor, offset=q * BLK * P + b * BLK,
                                  ap=[[1, BLK], [P, BLK], [1, BLK]])
                    sp.dma_start(toep[q * BLK:(q + 1) * BLK, :, b, q, :], src).then_inc(toep_in, 16)
            sp.wait_ge(toep_in, 192)

        @block.gpsimd
        def _(pool):
            nc.gpsimd.memset(toep[:, :, :, :, :], 0.0).then_inc(toep_zero, 1)

        @block.scalar
        def _(act):
            act.wait_ge(loaded, 64)
            nc.scalar.activation(dt_[:, :], cold[:, 0:1], ACT.Exp).then_inc(exps, 1)
            nc.scalar.activation(elr[:, :], lam[:, 0:NS], ACT.Exp).then_inc(exps, 1)
            act.wait_ge(args_done, 1)
            nc.scalar.activation(mag[:, :], ea[:, :, :, :].rearrange("p a b n -> p (a b n)"), ACT.Exp)
            act.wait_ge(args_done, 3)
            nc.scalar.activation(sc[:, :, :], ang[:, :, :], ACT.Sin).then_inc(trig_done, 1)
            for b in range(4):
                act.wait_ge(conv_mm, b + 1)
                nc.scalar.activation(y[:, :, 8 * b:8 * b + 8].rearrange("p t c -> p c t"),
                                     ps[:, b, :].rearrange("p (c t) -> p c t", c=8), ACT.Copy).then_inc(y_done, 1)

        @block.vector
        def _(dve):
            n = [0]
            v = nc.vector

            def link(ins):
                n[0] += 1
                ins.then_inc(chain, 1)
                dve.wait_ge(chain, n[0])

            v.memset(ut[:, 0:2, :], 0.0).then_inc(ut_done, 1)
            v.transpose(ut[:, 2:2 + NBLK, :],
                        g.za[:, 0:SEQ].rearrange("p (a b) -> p a b", b=BLK)[:, :, ::-1]).then_inc(ut_done, 1)
            dve.wait_ge(exps, 2)
            dve.wait_ge(loaded, 64)
            link(v.tensor_scalar(ab[:, 0, :], elr[:, :], dt_[:, 0:1], -1.0, ALU.mult, ALU.mult))
            link(v.tensor_scalar(ab[:, 1, :], lam[:, NS:2 * NS], dt_[:, 0:1], None, ALU.mult))
            st = steps[:, :, :, :].rearrange("p a b n -> p (a b) n")
            for part, dst in ((0, ea), (1, th)):
                v.tensor_tensor(dst[:, :, :, :].rearrange("p a b n -> p (a b) n"), st,
                                ab[:, part:part + 1, :].to_broadcast([P, 16, NS]), ALU.mult).then_inc(args_done, 1)
            dve.wait_ge(args_done, 2)
            t_ = th[:, :, :, :].rearrange("p a b n -> p (a b n)")
            for k, quarter in ((0, 0.0), (1, 0.25)):
                link(v.tensor_scalar(turns[:, k, :], t_, 1.0 / TWO_PI, quarter, ALU.mult, ALU.add))
            link(v.tensor_scalar(turns[:, :, :], turns[:, :, :], ROUND, None, ALU.add))
            link(v.tensor_scalar(turns[:, :, :], turns[:, :, :], -ROUND, None, ALU.add))
            for k in range(2):
                link(v.scalar_tensor_tensor(ang[:, k, :], turns[:, k, :], -TURN_HI, t_, ALU.mult, ALU.add))
            link(v.scalar_tensor_tensor(ang[:, :, :], turns[:, :, :], -TURN_LO, ang[:, :, :], ALU.mult, ALU.add))
            link(v.tensor_scalar(ang[:, 1, :], ang[:, 1, :], TWO_PI / 4, None, ALU.add))
            v.tensor_scalar(ang[:, :, :], ang[:, :, :], SIN_MAX, -SIN_MAX, ALU.min, ALU.max).then_inc(args_done, 1)
            dve.wait_ge(trig_done, 1)
            link(v.tensor_tensor(z[:, :, :, :, :].rearrange("p s a b n -> p s (a b n)"), sc[:, :, :],
                                 mag[:, :].rearrange("p (o n) -> p o n", o=1).to_broadcast([P, 2, 2 * 8 * NS]),
                                 ALU.mult))
            wre = prm[:, 0:NS].rearrange("p (o n) -> p o n", o=1).to_broadcast([P, 8, NS])
            wim = prm[:, NS:2 * NS].rearrange("p (o n) -> p o n", o=1).to_broadcast([P, 8, NS])
            for k, (w, s) in enumerate(((wre, 1), (wim, 0), (wre, 0), (wim, 1))):
                link(v.tensor_tensor(u[:, k, :, :], z[:, s, 1, :, :], w, ALU.mult))
            link(v.tensor_tensor(uw[:, 0, :, :], u[:, 0, :, :], u[:, 1, :, :], ALU.subtract))
            link(v.tensor_tensor(uw[:, 1, :, :], u[:, 2, :, :], u[:, 3, :, :], ALU.add))
            for k, dst in ((0, prod), (1, prod2)):
                for a in range(8):
                    ins = v.tensor_tensor(dst[:, a, :].rearrange("p (b n) -> p b n", b=8),
                                          z[:, 1 - k, 0, :, :],
                                          uw[:, k, a:a + 1, :].to_broadcast([P, 8, NS]), ALU.mult)
                link(ins)
            link(v.tensor_tensor(prod[:, :, :], prod[:, :, :], prod2[:, :, :], ALU.subtract))
            link(v.memset(pad[:, :], 0.0))
            link(v.tensor_reduce(taps[:, :].rearrange("p (a b) -> p a b", a=8),
                                 prod[:, :, :].rearrange("p a (b n) -> p a b n", b=8), AX.X, ALU.add))
            link(v.tensor_copy(pad[:, BLK - 1:BLK - 1 + LK], taps[:, :]))
            v.tensor_tensor(pad[:, BLK - 1:BLK], taps[:, 0:1], cold[:, 1:2], ALU.add).then_inc(pad_done, 1)
            dve.wait_ge(y_done, 4)
            link(v.transpose(yT[:, :], y[:, :, :].rearrange("p a b -> p (a b)")))
            v.tensor_tensor(g.x[:, :], g.x[:, :], yT[:, :], ALU.add)

        @block.tensor
        def _(pe):
            pe.wait_ge(ut_done, 2)
            pe.wait_ge(toep_in, 192)
            for ch in range(BLK):
                for b in range(3):
                    mm = nc.tensor.matmul(ps[:, ch // 8, (ch % 8) * NBLK:(ch % 8) * NBLK + NBLK],
                                          toep[:, ch, b, :, :].rearrange("p q t -> p (q t)"),
                                          ut[:, 2 - b:2 - b + NBLK, ch], start=(b == 0), stop=(b == 2))
                if ch % 8 == 7:
                    mm.then_inc(conv_mm, 1)

        block_end.close()
        clear(nc, sems)


def causal_phase(nc, g):
    JT = SEQ // P
    CPT = CH // P
    CHS = SEQ // CH
    ROWS = 6 * BD
    KR = ROWS + 3
    s_units = [(i, hf, min((i + 1) * P, (hf + 1) * 2 * CH) - hf * 2 * CH)
               for i in range(JT) for hf in range(2) if (i + 1) * P > hf * 2 * CH]
    t_units = [(ck, j, max(0, (j - CPT * ck) * P)) for ck in range(CHS) for j in range(CPT * ck + CPT)]
    last_of = {ck: n for n, (ck, j, i0) in enumerate(t_units)}
    NSU, NTU = len(s_units), len(t_units)
    NPT = 4
    sems = []
    with ExitStack() as c:
        def sb(n, shape, dt=F32):
            return c.enter_context(nc.sbuf_tensor("ca_" + n, shape, dt))

        def sem(n):
            return semaphore(nc, c, sems, "ca_" + n)

        wT = sb("wT", [P, 3 * P])
        woT = sb("woT", [P, P])
        bcol = sb("bcol", [P, 3])
        bv = sb("bv", [P, P])
        masks = sb("masks", [P, 2, P], BF16)
        full = sb("full", [P, 2, SEQ])
        rest = sb("rest", [P, SEQ])
        part = sb("part", [P, 2, 3, SEQ], BF16)
        va = sb("va", [P, JT, BH, BD + 1])
        vh = sb("vh", [P, 2, JT, BD + 1])
        qs = sb("qs", [P, 2, SEQ], BF16)
        ks = sb("ks", [P, 2, SEQ], BF16)
        mpart = sb("mpart", [P, 2, 2, JT])
        mx = sb("mx", [P, JT])
        nm = sb("nm", [JT, P])
        nmr = sb("nmr", [JT, P])
        mrow = sb("mrow", [JT, 3, P], BF16)
        pt = sb("pt", [P, NPT, CH])
        oa = sb("oa", [BD + 1, 2, SEQ])
        ctx = sb("ctx", [P, SEQ])
        den = sb("den", [P, SEQ])
        inv = sb("inv", [P, SEQ])
        ctxn = sb("ctxn", [P, SEQ])
        ps = c.enter_context(nc.psum_tensor("ca_ps", [P, 8, CH], F32))
        parts_d = nc.dram_tensor("parts_scratch", [2, 3, P, SEQ], BF16, kind="Internal").ap()
        ctx_d = nc.dram_tensor("ctx_scratch", [P, SEQ], F32, kind="Internal").ap()
        den_d = nc.dram_tensor("den_scratch", [BH, SEQ], F32, kind="Internal").ap()

        loaded, qk_mm, full_done = sem("loaded"), sem("qk_mm"), sem("full_done")
        split, parts_stored = sem("split"), sem("parts_stored")
        v_mm, v_done, ones_set = sem("v_mm"), sem("v_done"), sem("ones_set")
        heads_in = [sem("heads_in0"), sem("heads_in1")]
        m_in, vh_done = sem("m_in"), sem("vh_done")
        s_mm, max_done, mx_done, mT_mm = sem("s_mm"), sem("max_done"), sem("mx_done"), sem("mT_mm")
        m_split, mrow_done = sem("m_split"), sem("mrow_done")
        t_mm, exp_done, pv_mm, o_done = sem("t_mm"), sem("exp_done"), sem("pv_mm"), sem("o_done")
        o_stored, ctx_in, inv_done, ctx_done, y_mm = (sem("o_stored"), sem("ctx_in"), sem("inv_done"),
                                                      sem("ctx_done"), sem("y_mm"))
        block_end = c.enter_context(ExitStack())
        block = block_end.enter_context(nc.Block())

        def walk(eng, maxima, products):
            maxima(0, 0)
            products(0, 0, True)
            products(1, 1, True)
            with eng.Fori(1, BH // 2 - 1) as hp:
                products(hp * 2, 0, True)
                products(hp * 2 + 1, 1, True)
            products(BH - 2, 0, True)
            products(BH - 1, 1, False)

        def wait(eng, sm, value):
            if not isinstance(value, int) or value > 0:
                eng.wait_ge(sm, value)

        @block.sync
        def _(sp):
            for dst, src in ((wT[:, :], g.d["in_wT"]), (woT[:, :], g.d["out_wT"]), (bcol[:, :], g.d["b_cols"]),
                             (bv[:, :], g.d["b_v"].partition_broadcast(P)),
                             (masks[:, :, :], g.d["cmask"].rearrange("p (a b) -> p a b", a=2))):
                sp.dma_start(dst, src).then_inc(loaded, 16)
            for x in range(2):
                for k in range(3):
                    sp.wait_ge(split, 5 * x + 2 * k + 1)
                    sp.dma_start(parts_d[x, k], part[:, x, k, :]).then_inc(parts_stored, 16)
            def max_rows(head, e):
                sp.wait_ge(mrow_done, head + 1)
                for k in range(3):
                    sp.dma_start(qs[ROWS + k:ROWS + k + 1, e, :], mrow[:, k, :]).then_inc(m_in, 16)

            def maxima(head, e):
                max_rows(head, e)

            def products(head, e, more):
                if more:
                    max_rows(head + 1, 1 - e)

            walk(sp, maxima, products)
            sp.wait_ge(o_stored, 32 * BH)
            sp.dma_start(ctx[:, :], ctx_d).then_inc(ctx_in, 16)
            sp.dma_start(den[:, :], bass.AP(tensor=den_d.tensor, offset=0, ap=[[SEQ, BH], [0, BD], [1, SEQ]])
                         ).then_inc(ctx_in, 16)
            sp.wait_ge(ctx_in, 32)

        @block.gpsimd
        def _(pool):
            nc.gpsimd.memset(va[:, :, :, :], 1.0).then_inc(ones_set, 1)
            nc.gpsimd.memset(mpart[:, :, :, :], -3.0e38).then_inc(ones_set, 1)
            pool.wait_ge(ones_set, 2)
            nc.gpsimd.memset(ks[32:64, :, :], 1.0).then_inc(ones_set, 1)
            pool.wait_ge(v_done, 1)

            def stage(head, e):
                wait(pool, pv_mm, (head - 1) * NTU)
                nc.gpsimd.tensor_copy(vh[:, e, :, :], va[:, :, bass.ds(head, 1), :].rearrange(
                    "p j a d -> p j (a d)")).then_inc(vh_done, 1)

            def products(head, e, more):
                if more:
                    stage(head + 1, 1 - e)
                pool.wait_ge(o_done, CHS * (head + 1))
                pool.dma_start(ctx_d[bass.ds(head * BD, BD), :], oa[0:BD, e, :]).then_inc(o_stored, 16)
                pool.dma_start(den_d[bass.ds(head, 1), :], oa[BD:BD + 1, e, :]).then_inc(o_stored, 16)

            walk(pool, stage, products)

        @block.scalar
        def _(act):
            act.wait_ge(parts_stored, 96)
            act.wait_ge(ones_set, 3)

            def rows(x, k, step, n, head):
                r = parts_d[x, k, bass.ds(head * BD, BD), :]
                return bass.AP(tensor=r.tensor, offset=r.offset, ap=[[step * P * SEQ, n]] + list(r.ap))

            def load(head, e):
                wait(act, pv_mm, (head - 1) * NTU)
                for dst, x, k, step, n, at in ((qs, 0, 0, 0, 3, 0), (qs, 0, 1, 0, 2, 3), (qs, 0, 2, 0, 1, 5),
                                               (ks, 1, 0, 1, 3, 0), (ks, 1, 0, 1, 2, 3), (ks, 1, 0, 0, 1, 5)):
                    act.dma_start(dst[at * BD:(at + n) * BD, e, :], rows(x, k, step, n, head)).then_inc(heads_in[e], 16)

            def maxima(head, e):
                load(head, e)

            def products(head, e, more):
                if more:
                    load(head + 1, 1 - e)
                for n, (ck, j, i0) in enumerate(t_units):
                    k = head * NTU + n
                    act.wait_ge(t_mm, k + 1)
                    wait(act, pv_mm, k - NPT + 1 if n >= NPT else head * NTU)
                    nc.scalar.activation(pt[:, n % NPT, i0:CH], ps[:, 4 + n % 2, i0:CH], ACT.Exp
                                         ).then_inc(exp_done, 1)

            walk(act, maxima, products)

        @block.tensor
        def _(pe):
            pe.wait_ge(loaded, 80)
            for x in range(2):
                for b in range(4):
                    mm = nc.tensor.matmul(ps[:, 4 * x + b, :], wT[:, x * P:x * P + P], g.za[:, b * CH:b * CH + CH],
                                          start=True, stop=True)
                    mm.then_inc(qk_mm, 1)
            pe.wait_ge(full_done, 4)
            for t in range(JT):
                mm = nc.tensor.matmul(ps[:, t // 4, (t % 4) * P:(t % 4) * P + P], g.za[:, t * P:t * P + P],
                                      wT[:, 2 * P:3 * P], start=True, stop=True)
            mm.then_inc(v_mm, 1)
            pe.wait_ge(v_done, 1)
            pe.wait_ge(full_done, 8)

            def score(head, e, n):
                i, hf, cols = s_units[n]
                k = head * NSU + n
                slot = 2 * (n % 2)
                if n >= 2 or not isinstance(head, int) or head > 0:
                    pe.wait_ge(max_done, k - 1)
                for c0 in range(0, cols, CH):
                    w = min(CH, cols - c0)
                    diag = hf * 2 * CH + c0 + w == (i + 1) * P
                    mm = nc.tensor.matmul(ps[:, slot + c0 // CH, 0:w], qs[0:ROWS, e, i * P:i * P + P],
                                          ks[0:ROWS, e, hf * 2 * CH + c0:hf * 2 * CH + c0 + w],
                                          start=True, stop=not diag, skip_group_check=True)
                    if diag:
                        mm = nc.tensor.matmul(ps[:, slot + c0 // CH, w - P:w], g.identb[:, :], masks[:, 0, :],
                                              start=False, stop=True, skip_group_check=True)
                mm.then_inc(s_mm, 1)

            def turn_max(head, e):
                pe.wait_ge(mx_done, head + 1)
                wait(pe, mrow_done, head)
                nc.tensor.transpose(ps[0:JT, 7, 0:P], mx[:, :], g.ident[:, :]).then_inc(mT_mm, 1)

            def maxima(head, e):
                pe.wait_ge(heads_in[e], 48 * (head - e) + 96)
                for n in range(NSU):
                    score(head, e, n)
                turn_max(head, e)

            def products(head, e, more):
                pe.wait_ge(m_in, 48 * (head + 1))
                pe.wait_ge(vh_done, head + 1)
                done = 0

                def pv(n):
                    ck, j, i0 = t_units[n]
                    pe.wait_ge(exp_done, head * NTU + n + 1)
                    if j == 0:
                        wait(pe, o_done, head * CHS + ck)
                    mm = nc.tensor.matmul(ps[0:BD + 1, 6, i0:CH], vh[:, e, j, :], pt[:, n % NPT, i0:CH],
                        start=(j == 0), stop=(j == CPT * ck + CPT - 1), skip_group_check=True)
                    mm.then_inc(pv_mm, 1)

                for n, (ck, j, i0) in enumerate(t_units):
                    k = head * NTU + n
                    wait(pe, exp_done, k - 1 if n >= 2 else head * NTU)
                    diag = j >= CPT * ck
                    mm = nc.tensor.matmul(ps[:, 4 + n % 2, i0:CH], ks[0:KR, e, j * P:j * P + P],
                                          qs[0:KR, e, ck * CH + i0:ck * CH + CH],
                                          start=True, stop=not diag, skip_group_check=True)
                    if diag:
                        mm = nc.tensor.matmul(ps[:, 4 + n % 2, i0:i0 + P], g.identb[:, :], masks[:, 1, :],
                                              start=False, stop=True, skip_group_check=True)
                    mm.then_inc(t_mm, 1)
                    if more:
                        while done < NSU and done * NTU < (n + 1) * NSU:
                            if done == 0:
                                pe.wait_ge(heads_in[1 - e], 48 * (head + e) + 96)
                            score(head + 1, 1 - e, done)
                            done += 1
                    if n > 0:
                        pv(n - 1)
                pv(NTU - 1)
                if more:
                    turn_max(head + 1, 1 - e)

            walk(pe, maxima, products)
            for b in range(4):
                pe.wait_ge(ctx_done, b + 1)
                nc.tensor.matmul(ps[:, b, :], woT[:, :], ctxn[:, b * CH:b * CH + CH], start=True, stop=True
                                 ).then_inc(y_mm, 1)

        @block.vector
        def _(dve):
            v = nc.vector
            dve.wait_ge(loaded, 80)
            for x in range(2):
                for b in range(4):
                    dve.wait_ge(qk_mm, 4 * x + b + 1)
                    v.tensor_scalar(full[:, x, b * CH:b * CH + CH], ps[:, 4 * x + b, :], bcol[:, x:x + 1],
                                    float(BD) ** -0.5 if x == 0 else 1.0, ALU.add, ALU.mult).then_inc(full_done, 1)
            for x in range(2):
                n = 5 * x
                dve.wait_ge(full_done, 4 * x + 4)
                dve.wait_ge(split, n) if n else None
                v.tensor_copy(part[:, x, 0, :], full[:, x, :]).then_inc(split, 1)
                dve.wait_ge(split, n + 1)
                v.tensor_tensor(full[:, x, :], full[:, x, :], part[:, x, 0, :], ALU.subtract).then_inc(split, 1)
                dve.wait_ge(split, n + 2)
                v.tensor_copy(part[:, x, 1, :], full[:, x, :]).then_inc(split, 1)
                dve.wait_ge(split, n + 3)
                v.tensor_tensor(rest[:, :], full[:, x, :], part[:, x, 1, :], ALU.subtract).then_inc(split, 1)
                dve.wait_ge(split, n + 4)
                v.tensor_copy(part[:, x, 2, :], rest[:, :]).then_inc(split, 1)
            dve.wait_ge(v_mm, 1)
            dve.wait_ge(ones_set, 3)
            for b in range(4):
                for t in range(4):
                    last = v.tensor_tensor(va[:, 4 * b + t, :, 0:BD],
                                           ps[:, b, t * P:t * P + P].rearrange("p (h d) -> p h d", h=BH),
                                           bv[:, :].rearrange("p (h d) -> p h d", h=BH), ALU.add)
            last.then_inc(v_done, 1)

            def reduce(head, e, n):
                i, hf, cols = s_units[n]
                dve.wait_ge(s_mm, head * NSU + n + 1)
                slot = 2 * (n % 2)
                v.tensor_reduce(mpart[:, e, hf, i:i + 1],
                                ps[:, slot:slot + 2, :].rearrange("p a b -> p (a b)")[:, 0:cols], AX.X, ALU.max
                                ).then_inc(max_done, 1)

            def finish_max(head, e):
                dve.wait_ge(max_done, NSU * (head + 1))
                wait(dve, mT_mm, head)
                v.tensor_tensor(mx[:, :], mpart[:, e, 0, :], mpart[:, e, 1, :], ALU.max).then_inc(mx_done, 1)
                dve.wait_ge(mT_mm, head + 1)
                wait(dve, m_in, 48 * head)
                ms = 4 * head
                v.tensor_scalar(nm[:, :], ps[0:JT, 7, 0:P], -1.0, None, ALU.mult).then_inc(m_split, 1)
                dve.wait_ge(m_split, ms + 1)
                v.tensor_copy(mrow[:, 0, :], nm[:, :]).then_inc(m_split, 1)
                dve.wait_ge(m_split, ms + 2)
                v.tensor_tensor(nmr[:, :], nm[:, :], mrow[:, 0, :], ALU.subtract).then_inc(m_split, 1)
                dve.wait_ge(m_split, ms + 3)
                v.tensor_copy(mrow[:, 1, :], nmr[:, :]).then_inc(m_split, 1)
                dve.wait_ge(m_split, ms + 4)
                v.tensor_tensor(mrow[:, 2, :], nmr[:, :], mrow[:, 1, :], ALU.subtract).then_inc(mrow_done, 1)

            def maxima(head, e):
                for n in range(NSU):
                    reduce(head, e, n)
                finish_max(head, e)

            def products(head, e, more):
                done = 0
                for n, (ck, j, i0) in enumerate(t_units):
                    if more:
                        while done < NSU and done * NTU < (n + 1) * NSU:
                            reduce(head + 1, 1 - e, done)
                            done += 1
                    if j == CPT * ck + CPT - 1 and n < NTU - 1:
                        copy_out(head, e, ck)
                copy_out(head, e, CHS - 1)
                if more:
                    finish_max(head + 1, 1 - e)

            def copy_out(head, e, ck):
                dve.wait_ge(pv_mm, head * NTU + last_of[ck] + 1)
                wait(dve, o_stored, 32 * head)
                v.tensor_copy(oa[:, e, ck * CH:ck * CH + CH], ps[0:BD + 1, 6, :]).then_inc(o_done, 1)

            walk(dve, maxima, products)
            dve.wait_ge(ctx_in, 32)
            for b in range(4):
                s = slice(b * CH, b * CH + CH)
                v.reciprocal(inv[:, s], den[:, s]).then_inc(inv_done, 1)
                dve.wait_ge(inv_done, b + 1)
                v.tensor_tensor(ctxn[:, s], ctx[:, s], inv[:, s], ALU.mult).then_inc(ctx_done, 1)
            for b in range(4):
                s = slice(b * CH, b * CH + CH)
                dve.wait_ge(y_mm, b + 1)
                v.scalar_tensor_tensor(g.x[:, s], ps[:, b, :], bcol[:, 2:3], g.x[:, s], ALU.add, ALU.add)

        block_end.close()
        clear(nc, sems)


def store_phase(nc, g, out):
    sems = []
    with ExitStack() as c:
        stored = semaphore(nc, c, sems, "stored")
        block_end = c.enter_context(ExitStack())
        block = block_end.enter_context(nc.Block())

        @block.sync
        def _(sp):
            sp.dma_start(out, g.x[:, :]).then_inc(stored, 16)
            sp.wait_ge(stored, 16)

        block_end.close()
        clear(nc, sems)


def build(nc, d, out, phases="AFBF"):
    g = Shared()
    g.d = d
    sems = []
    with ExitStack() as c:
        def sb(n, shape, dt=F32):
            return c.enter_context(nc.sbuf_tensor(n, shape, dt))

        g.x = sb("x_stream", [P, SEQ])
        g.za = sb("za", [P, SEQ + 1])
        g.zb = sb("zb", [P, SEQ + 1])
        g.ident = sb("ident", [P, P])
        g.identb = sb("identb", [P, P], BF16)
        g.mean_w = sb("mean_w", [P, P])
        g.eps = sb("eps", [P, 1])
        load_phase(nc, g)
        for n, ph in enumerate(phases):
            norm_phase(nc, g, f"n{n}", ph == "F")
            if ph == "A":
                conv_phase(nc, g)
            elif ph == "B":
                causal_phase(nc, g)
            else:
                stack_phase(nc, g, f"f{n}")
        store_phase(nc, g, out)


def constants():
    bfloat16 = mybir.dt.np(BF16)
    half = np.arange(0, DH, 2, dtype=np.float32)
    inv_freq = (1.0 / np.float32(10000.0) ** (half / np.float32(DH))).astype(np.float32)
    t = np.arange(SEQ, dtype=np.float32)
    freqs = (t[:, None] * inv_freq[None, :]).astype(np.float32).astype(np.float64)
    base = (half.astype(np.float64) + 0.4 * DH) / (1.4 * DH)
    power = (np.arange(SEQ) % P) / (WIN // 2)
    scale = base[None, :] ** power[:, None]
    cos, sin = np.cos(freqs), np.sin(freqs)
    two = lambda a, b: np.concatenate([a, b], 1)
    tabs = [two(cos * scale, cos * scale) * 8.0, two(-sin * scale, sin * scale) * 8.0,
            two(cos / scale, cos / scale), two(-sin / scale, sin / scale)]
    rope = np.stack(tabs, 1).reshape(TILES, P, 4 * DH).transpose(1, 0, 2).reshape(P, -1).astype(np.float32)
    carry = np.tile(np.concatenate([base, base]) ** (P / (WIN // 2)), 2)[:, None].astype(np.float32)
    i = np.arange(WIN)[:, None]
    j = np.arange(2 * WIN)[None, :]
    usual = np.tile(np.where((j >= i) & (j <= i + WIN), 0.0, MASKED), (4, 2))
    first = usual.copy()
    first[0:64, 0:WIN] = MASKED
    q = np.arange(P)
    return {
        "rope": rope, "carry": carry,
        "mask": np.concatenate([usual, first], 1).astype(bfloat16),
        "ident": np.eye(P, dtype=np.float32), "identb": np.eye(P, dtype=bfloat16),
        "steps": np.concatenate([np.repeat(np.arange(8), NS), np.repeat(8 * np.arange(8), NS)]).astype(np.float32),
        "cmask": np.concatenate([np.where(q[None, :] > q[:, None], MASKED, 0.0),
                                 np.where(q[:, None] > q[None, :], MASKED, 0.0)], 1).astype(bfloat16),
    }


_INS = {"x": "L0_attn_a_u", "D": "L0_attn_a_D", "Lambda_re": "L0_attn_a_Lambda_re",
        "Lambda_im": "L0_attn_a_Lambda_im", "log_dt": "L0_attn_a_log_dt", "W_re": "L0_attn_a_W_re",
        "W_im": "L0_attn_a_W_im", "in_proj_w": "L0_attn_b_in_proj_w", "in_proj_b": "L0_attn_b_in_proj_b",
        "out_proj_w": "L0_attn_b_out_proj_w", "out_proj_b": "L0_attn_b_out_proj_b", "Wqkv": "L0_ffn_Wqkv",
        "q_scale": "L0_ffn_q_scale", "k_scale": "L0_ffn_k_scale", "Wo": "L0_ffn_Wo", "ln_g": "L0_ffn_ln_g",
        "ln_b": "L0_ffn_ln_b", "W1": "L0_ffn_W1", "b1": "L0_ffn_b1", "W2": "L0_ffn_W2", "b2": "L0_ffn_b2"}


def layout(inputs):
    a = {k: np.asarray(inputs[v]) for k, v in _INS.items()}
    out = {k: a[k] for k in ("Wqkv", "Wo", "W1", "W2")}
    out["x"] = a["x"][0].T
    for k in ("b2", "ln_g", "ln_b"):
        out[k] = a[k].T
    b1 = np.zeros((P, DEPTH, 2, NCH), a["b1"].dtype)
    for part in range(2):
        for j, (f0, fn) in enumerate(FCH):
            b1[0:fn, :, part, j] = a["b1"][:, part * FF + f0:part * FF + f0 + fn].T
    out["b1"] = b1.reshape(P, -1)
    half = DH // 2
    swap = lambda s: np.concatenate([s[:, half:], s[:, :half]], 1)
    out["qk_scale"] = np.stack([a["q_scale"], swap(a["q_scale"]), a["k_scale"], swap(a["k_scale"])], 1)
    out["W_ri"] = np.concatenate([a["W_re"], a["W_im"]], 1)
    out["lam"] = np.concatenate([a["Lambda_re"], a["Lambda_im"]])
    out["dt_D"] = np.stack([a["log_dt"], a["D"]], 1)
    out["in_wT"] = a["in_proj_w"].T
    out["out_wT"] = a["out_proj_w"].T
    out["b_cols"] = np.stack([a["in_proj_b"][0:P], a["in_proj_b"][P:2 * P], a["out_proj_b"]], 1)
    out["b_v"] = a["in_proj_b"][2 * P:3 * P]
    out.update(constants())
    return {k: np.ascontiguousarray(v) for k, v in out.items()}


def kernel(**inputs):
    import concourse.bacc as _bacc
    from concourse import mybir as _mybir
    from concourse.bass_utils import run_bass_kernel_spmd as _run

    nc = _bacc.Bacc("TRN2", target_bir_lowering=False, num_devices=1)
    arrays, d = {}, {}
    for k, a in layout(inputs).items():
        arrays[f"in_{k}"] = a
        d[k] = nc.dram_tensor(f"in_{k}", a.shape, _mybir.dt.from_np(a.dtype), kind="ExternalInput").ap()
    out = nc.dram_tensor("out", (P, SEQ), _mybir.dt.float32, kind="ExternalOutput").ap()
    build(nc, d, out)
    r = _run(nc, [arrays], core_ids=[0])
    return np.ascontiguousarray(r.results[0]["out"].T)[None]
```
